# Optimizing a Trainium2 kernel written in Bass

```python
import numpy as np
import jax
import jax.numpy as jnp

def _softmax(x, axis=-1):
    return jax.nn.softmax(x, axis=axis)

def _gelu(x):
    return jax.nn.gelu(x, approximate=True)

def _silu(x):
    return jax.nn.silu(x)

def _sigmoid(x):
    return jax.nn.sigmoid(x)

def _layernorm(x, axis=-1, eps=1e-05):
    m = jnp.mean(x, axis=axis, keepdims=True)
    v = jnp.var(x, axis=axis, keepdims=True)
    return (x - m) / jnp.sqrt(v + eps)

def _scatter_add(tgt, idx, src, axis=0):
    return tgt.at[idx].add(src)

def _segment_sum(src, seg, n):
    return jax.ops.segment_sum(src, seg, n)
kernel_name = 'mk_adj_preln_d1_adj_r2_b4b1c4'

def setup_inputs(seed: int=0):
    np.random.seed(seed)
    _w = jnp.asarray

    def _rec_inputs():
        import jax
        import jax.numpy as jnp
        _gk = jax.random.key(seed)
        x = 7.22e-05 + 1 * jax.random.normal(jax.random.fold_in(_gk, 1), (8, 2048, 128), jnp.float32)
        _a = jax.random.bernoulli(jax.random.fold_in(_gk, 2), 0.00390625, (2048, 2048))
        _a = jnp.logical_or(_a, jnp.swapaxes(_a, -1, -2))
        _a = jnp.logical_or(_a, jnp.eye(2048, dtype=bool))
        _af = _a.astype(jnp.float32)
        _af = _af * jax.random.uniform(jax.random.fold_in(_gk, 3), (2048, 2048), jnp.float32, 0.05, 0.119748)
        adj = _af
        return (x, adj)
    x, adj = _rec_inputs()

    def _L0_gnn_setup():
        import jax, jax.numpy as jnp
        import numpy as np
        B, N, F_IN, F_OUT = (8, 2048, 128, 128)
        key = jax.random.key(seed)
        k1, k2, k3 = jax.random.split(key, 3)
        H = jax.random.normal(k1, (B, N, F_IN), dtype=jnp.float32)
        W = jax.random.normal(k2, (F_IN, F_OUT), dtype=jnp.float32) * (1.0 / np.sqrt(F_IN))
        A = jax.random.normal(k3, (N, N), dtype=jnp.float32) * (1.414 * np.sqrt(2.0 / (N + N)))
        return {'H': H, 'W': W, 'A': A}
    _L0_gnn_all = _L0_gnn_setup()
    _L0_gnn_in = {k: v for k, v in _L0_gnn_all.items() if k in ('W',)}
    del _L0_gnn_all
    return {'x': x, 'adj': adj, 'L0_gnn_W': _L0_gnn_in['W']}

def reference(x, adj, L0_gnn_W):
    import jax
    import jax.numpy as jnp

    def _L0_gnn_ref(H, W, A):
        import jax, jax.numpy as jnp
        import numpy as np
        B, N, F_IN, F_OUT = (8, 2048, 128, 128)
        HW = jnp.einsum('bnf,fo->bno', H, W)
        A_norm = jax.nn.relu((A + A.T) * 0.5)
        D = jnp.sum(A_norm, axis=1)
        D_safe = jnp.where(D > 0, D, 1.0)
        d_inv_sqrt = jnp.where(D > 0, D_safe ** (-0.5), 0.0)
        DAD = d_inv_sqrt[:, None] * A_norm * d_inv_sqrt[None, :]
        L_norm = jnp.eye(N, dtype=H.dtype) - DAD
        out = jnp.einsum('nm,bmo->bno', L_norm, HW)
        return jax.nn.relu(out)
    h = jnp.maximum(_layernorm(x, axis=-1), 0.0)
    x = x + _L0_gnn_ref(h, L0_gnn_W, adj)
    return x

_drawn_inputs = setup_inputs


def setup_inputs(seed=0):
    import zlib

    import numpy as np

    out = dict(_drawn_inputs(seed))
    spreads = {}
    factors = {}
    for name, (base, spread) in spreads.items():
        noise = np.random.default_rng([zlib.crc32(name.encode()), seed]).standard_normal(out[name].shape)
        drawn = base * np.exp(spread * noise) if base else spread * noise
        out[name] = jnp.asarray(drawn.astype(out[name].dtype))
    for name, factor in factors.items():
        out[name] = (out[name] * factor).astype(out[name].dtype)
    return out
```

```python
from contextlib import ExitStack

import concourse.bass as bass
from concourse import mybir

ALU = mybir.AluOpType
ACT = mybir.ActivationFunctionType
F32 = mybir.dt.float32
F16 = mybir.dt.float16

P = 128
LN_EPS = 1e-5
LO_UP = 2048.0
G_UP = 512.0


def gnn_kernel(nc: bass.Bass, x: bass.AP, adj: bass.AP, W: bass.AP, out: bass.AP):
    B, N, F = x.shape
    NB = N // P
    CW = 512
    BPC = CW // P
    NCH = N // CW
    ROWS, COLS, XLN, DIAG = 3, 2, 5, 3
    HALF = NB // 2
    assert F == P and B % 2 == 0 and NB % BPC == 0

    row_at, col_at, at = [], [], 0
    for s in range(ROWS):
        row_at.append(at)
        at += (NB - s) * P
    for s in range(COLS):
        col_at.append(at)
        at += (NB - 1 - s) * P
    STAGE = at

    def blocks_of(first):
        return [(j, min(BPC, NB - j)) for j in range(first, NB, BPC)]

    t_before = [sum(len(blocks_of(s)) for s in range(k)) for k in range(NB + 1)]
    f_before = [sum(len(blocks_of(s + 1)) for s in range(k)) for k in range(NB + 1)]

    with ExitStack() as ctx:
        def sb(name, shape, dt):
            return ctx.enter_context(nc.sbuf_tensor(name, shape, dt))

        def psum(name, shape, dt):
            return ctx.enter_context(nc.psum_tensor(name, shape, dt))

        def sem(name):
            return ctx.enter_context(nc.semaphore(name))

        mat = sb("mat", [P, NB, 2, N], F16)
        stage = sb("stage", [P, STAGE], F32)
        xln = sb("xln", [P, XLN, 2, F], F32)
        g = sb("g", [P, 2, NB, 3, F], F16)
        diag = sb("diag", [P, DIAG, P], F32)
        norm2 = sb("norm2", [P, 2, F], F32)
        w_sb = sb("w_sb", [F, F], F32)
        ident = sb("ident", [P, P], F32)
        ident16 = sb("ident16", [P, P], F16)
        ones_hi = sb("ones_hi", [P, 1], F16)
        ones_lo = sb("ones_lo", [P, 1], F16)
        minus_half = sb("minus_half", [P, NB], F32)
        rowacc = sb("rowacc", [P, NB], F32)
        deg = sb("deg", [P, NB], F32)
        stats2 = sb("stats2", [P, NB, 2, 6], F32)
        mv2 = sb("mv2", [P, NB, 2, 2], F32)
        pre3 = sb("pre3", [P, NB, 3], F32)
        inv3 = sb("inv3", [P, NB, 3], F32)
        gain2 = sb("gain2", [P, NB, 2], F32)
        y_in = sb("y_in", [P, NB], F32)
        y_out = sb("y_out", [P, NB], F32)
        stats = sb("stats", [P, NB, 6], F32)
        mv = sb("mv", [P, NB, 2], F32)
        veps = sb("veps", [P, NB], F32)
        rstd = sb("rstd", [P, NB], F32)
        gain = sb("gain", [P, NB], F32)

        xs = stage[:, 0:2 * NB * F].rearrange("p (b t f) -> p b t f", b=2, t=NB)
        at = 2 * NB * F
        norm = stage[:, at:at + NB * F].rearrange("p (t f) -> p t f", t=NB)
        at += NB * F
        u_sb = stage[:, at:at + 2 * CW].rearrange("p (s n) -> p s n", s=2)
        at += 2 * CW
        o_sb = stage[:, at:at + 2 * CW].rearrange("p (s t f) -> p s t f", s=2, f=F)

        acc = psum("acc", [P, NCH, CW], F32)
        tp = psum("tp", [P, 2, CW], F32)
        ft = psum("ft", [P, BPC, 2, P], F16)
        dps = psum("dps", [P, CW], F32)

        ident_zero = sem("ident_zero")
        ident_done = sem("ident_done")
        ident16_done = sem("ident16_done")
        consts_done = sem("consts_done")
        w_here = sem("w_here")
        row_here = [sem(f"row_here{s}") for s in range(ROWS)]
        col_here = [sem(f"col_here{s}") for s in range(COLS)]
        xln_here = [sem(f"xln_here{s}") for s in range(XLN)]
        piece_here = [sem(f"piece_here{i}") for i in range(NCH)]
        adjT_ready = sem("adjT_ready")
        sum_done = sem("sum_done")
        relu_done = sem("relu_done")
        hi_done = sem("hi_done")
        lo_done = sem("lo_done")
        colsum_done = sem("colsum_done")
        deg_done = sem("deg_done")
        stats2_done = sem("stats2_done")
        mv2_done = sem("mv2_done")
        pre3_done = sem("pre3_done")
        inv3_done = sem("inv3_done")
        gain2_done = sem("gain2_done")
        norm2_done = sem("norm2_done")
        ghi2_done = sem("ghi2_done")
        glo2_done = sem("glo2_done")
        gneg2_done = sem("gneg2_done")
        diag_copied = sem("diag_copied")
        diag_done = sem("diag_done")
        diag_hi_done = sem("diag_hi_done")
        shell_done = sem("shell_done")
        matT_ready = sem("matT_ready")
        matT_stored = sem("matT_stored")
        y_done = sem("y_done")
        x_here = [sem(f"x_here{s}") for s in range(2)]
        acc_ready = sem("acc_ready")
        u_ready = sem("u_ready")
        uw_ready = sem("uw_ready")
        relu_out_done = sem("relu_out_done")
        add_done = sem("add_done")
        stored = [sem(f"stored{s}") for s in range(2)]
        stats_done = sem("stats_done")
        mv_done = sem("mv_done")
        veps_done = sem("veps_done")
        rstd_done = sem("rstd_done")
        gain_done = sem("gain_done")
        norm_done = sem("norm_done")
        ghi_done = sem("ghi_done")
        glo_done = sem("glo_done")
        gneg_done = sem("gneg_done")

        x_blocks = x.rearrange("b (t p) f -> b p t f", p=P)
        out_blocks = out.rearrange("b (t p) f -> b p t f", p=P)

        def row_part(k, j, n):
            o = row_at[k % ROWS] + (j - k) * P
            return stage[:, o:o + n * P]

        def col_part(k, j):
            o = col_at[k % COLS] + (j - k - 1) * P
            return stage[:, o:o + P]

        def row_loads(k):
            return k // ROWS + (k % ROWS != 0)

        def col_loads(k):
            return k // COLS + (k % COLS != 0)

        block = ctx.enter_context(nc.Block())

        @block.sync
        def _(sp):
            def load_shell(k):
                if k >= ROWS:
                    sp.wait_ge(lo_done, k - ROWS + 1)
                    sp.wait_ge(diag_copied, k - ROWS + 1)
                sp.dma_start(row_part(k, k, NB - k), adj[k * P:(k + 1) * P, k * P:N]).then_inc(row_here[k % ROWS], 16)
                if k + 1 < NB:
                    if k >= COLS:
                        sp.wait_ge(adjT_ready, t_before[k - COLS + 1])
                    dst = stage[:, col_at[k % COLS]:col_at[k % COLS] + (NB - 1 - k) * P]
                    sp.dma_start(dst.rearrange("p (j c) -> p j c", c=P),
                                 adj[(k + 1) * P:N, k * P:(k + 1) * P].rearrange("(j p) c -> p j c", p=P)
                                 ).then_inc(col_here[k % COLS], 16)
                load_xln(k)

            def load_xln(k):
                if k >= XLN:
                    sp.wait_ge(norm2_done, 2 * (k - XLN + 1))
                sp.dma_start(xln[:, k % XLN], x[0:2, k * P:(k + 1) * P, :].rearrange("b p f -> p b f")
                             ).then_inc(xln_here[k % XLN], 16)

            for i, (j, n) in enumerate(blocks_of(0)):
                sp.dma_start(row_part(0, j, n), adj[0:P, j * P:(j + n) * P]).then_inc(piece_here[i], 16)
                jc, nc_ = (1, n - 1) if j == 0 else (j, n)
                dst = stage[:, col_at[0] + (jc - 1) * P:col_at[0] + (jc - 1 + nc_) * P]
                sp.dma_start(dst.rearrange("p (j c) -> p j c", c=P),
                             adj[jc * P:(jc + nc_) * P, 0:P].rearrange("(j p) c -> p j c", p=P)
                             ).then_inc(piece_here[i], 16)
                if i == 0:
                    load_xln(0)
            for k in range(1, NB):
                load_shell(k)
                if k == 1:
                    sp.dma_start(w_sb[:, :], W).then_inc(w_here, 16)
            def load_x(b, par):
                for h in range(2):
                    ts = slice(h * HALF, (h + 1) * HALF)
                    sp.dma_start(xs[:, par, ts, :], x_blocks[b, :, ts, :]).then_inc(x_here[par], 16)

            sp.wait_ge(shell_done, NB)
            load_x(0, 0)
            load_x(1, 1)

            def store(b, j, par):
                sp.wait_ge(add_done, NCH * b + j + 1)
                sp.dma_start(out_blocks[b, :, j * BPC:(j + 1) * BPC, :], o_sb[:, par]).then_inc(stored[par], 16)

            for j in range(NCH):
                store(0, j, j % 2)

            with sp.Fori(0, B // 2 - 1) as i:
                for b, par in ((2 * i + 1, 1), (2 * i + 2, 0)):
                    sp.wait_ge(add_done, NCH * b)
                    load_x(b + 1, 1 - par)
                    for j in range(NCH):
                        store(b, j, j % 2)
            for j in range(NCH):
                store(B - 1, j, j % 2)
            for s in range(2):
                sp.wait_ge(stored[s], 16 * B * NCH // 2)

        @block.gpsimd
        def _(pool):
            nc.gpsimd.memset(ident[:, :], 0.0).then_inc(ident_zero, 1)
            pool.wait_ge(ident_zero, 1)
            nc.gpsimd.affine_select(out=ident[:, :], in_=ident[:, :], compare_op=ALU.not_equal, fill=1.0,
                                    base=0, pattern=[[-1, P]], channel_multiplier=1).then_inc(ident_done, 1)
            nc.gpsimd.memset(ones_hi[:, :], -LO_UP).then_inc(consts_done, 1)
            nc.gpsimd.memset(ones_lo[:, :], 1.0).then_inc(consts_done, 1)
            nc.gpsimd.memset(minus_half[:, :], -0.5).then_inc(consts_done, 1)
            pool.wait_ge(consts_done, 3)

            def copy_diag(k):
                pool.wait_ge(relu_done, k + 1)
                if k >= DIAG:
                    pool.wait_ge(shell_done, k - DIAG + 1)
                nc.gpsimd.tensor_copy(diag[:, k % DIAG, :], row_part(k, k, 1)).then_inc(diag_copied, 1)

            copy_diag(0)
            for k in range(NB):
                pool.wait_ge(mv2_done, k + 1)
                nc.gpsimd.tensor_scalar(pre3[:, k, 0:2], mv2[:, k, :, 1], LN_EPS, None, ALU.add
                                        ).then_inc(pre3_done, 1)
                pool.wait_ge(deg_done, k + 1)
                nc.gpsimd.tensor_scalar(pre3[:, k, 2:3], deg[:, k:k + 1], 0.0, deg[:, k:k + 1], ALU.is_le, ALU.add
                                        ).then_inc(pre3_done, 1)
                pool.wait_ge(pre3_done, 2 * k + 2)
                nc.gpsimd.tensor_tensor(inv3[:, k, :], pre3[:, k, :], minus_half[:, 0:3], ALU.pow
                                        ).then_inc(inv3_done, 1)
                pool.wait_ge(inv3_done, k + 1)
                nc.gpsimd.tensor_scalar(gain2[:, k, :], inv3[:, k, 0:2], inv3[:, k, 2:3], G_UP, ALU.mult, ALU.mult
                                        ).then_inc(gain2_done, 1)
                pool.wait_ge(ghi2_done, k + 1)
                nc.gpsimd.tensor_scalar(g[:, :, k, 2, :], g[:, :, k, 0, :], -1.0 / LO_UP, 1.0, ALU.mult, ALU.mult
                                        ).then_inc(gneg2_done, 1)
                if k + 1 < NB:
                    copy_diag(k + 1)
            nc.gpsimd.tensor_scalar(y_in[:, :], inv3[:, :, 2], G_UP, 1.0, ALU.mult, ALU.mult).then_inc(y_done, 1)
            nc.gpsimd.tensor_scalar(y_out[:, :], inv3[:, :, 2], LO_UP / G_UP, 1.0, ALU.mult, ALU.mult
                                    ).then_inc(y_done, 1)
            pool.wait_ge(y_done, 2)

            def add_x(b, j, par):
                pool.wait_ge(relu_out_done, NCH * b + j + 1)
                o = o_sb[:, j % 2]
                nc.gpsimd.tensor_tensor(o, o, xs[:, par, j * BPC:(j + 1) * BPC, :], ALU.add).then_inc(add_done, 1)

            def gains(b):
                pool.wait_ge(mv_done, b - 1)
                nc.gpsimd.nop(nofuse=True)
                nc.gpsimd.tensor_scalar(veps[:, :], mv[:, :, 1], LN_EPS, None, ALU.add).then_inc(veps_done, 1)
                pool.wait_ge(veps_done, b - 1)
                nc.gpsimd.tensor_tensor(rstd[:, :], veps[:, :], minus_half[:, :], ALU.pow).then_inc(rstd_done, 1)
                pool.wait_ge(rstd_done, b - 1)
                nc.gpsimd.tensor_tensor(gain[:, :], rstd[:, :], y_in[:, :], ALU.mult).then_inc(gain_done, 1)

            def g_neg(b, h, par):
                pool.wait_ge(glo_done, 2 * (b - 2) + h + 1)
                nc.gpsimd.nop(nofuse=True)
                t = slice(h * HALF, (h + 1) * HALF)
                nc.gpsimd.tensor_scalar(g[:, par, t, 2, :], g[:, par, t, 0, :], -1.0 / LO_UP, 1.0,
                                        ALU.mult, ALU.mult).then_inc(gneg_done, 1)

            pool.wait_ge(x_here[0], 32)
            for j in range(NCH - 1):
                add_x(0, j, 0)

            with pool.Fori(0, B // 2 - 1) as i:
                for b, par in ((2 * i + 1, 1), (2 * i + 2, 0)):
                    add_x(b - 1, NCH - 1, 1 - par)
                    gains(b + 1)
                    pool.wait_ge(x_here[par], 32 * (i + 2 - par))
                    add_x(b, 0, par)
                    g_neg(b + 1, 0, 1 - par)
                    add_x(b, 1, par)
                    g_neg(b + 1, 1, 1 - par)
                    add_x(b, 2, par)
            add_x(B - 2, NCH - 1, 0)
            for j in range(NCH):
                add_x(B - 1, j, 1)

        @block.vector
        def _(dve):
            def sums(k, first=0, last=NCH):
                for i, (j, n) in list(enumerate(blocks_of(k)))[first:last]:
                    c = t_before[k] + i
                    if k == 0:
                        dve.wait_ge(piece_here[i], 32)
                    elif i == 0:
                        dve.wait_ge(row_here[k % ROWS], 16 * row_loads(k))
                    dve.wait_ge(adjT_ready, c + 1)
                    nc.vector.tensor_tensor(row_part(k, j, n), row_part(k, j, n), tp[:, c % 2, 0:n * P], ALU.add
                                            ).then_inc(sum_done, 1)

            def statistics2(k):
                dve.wait_ge(xln_here[k % XLN], 16 * (k // XLN + 1))
                for b in range(2):
                    nc.vector.bn_stats(stats2[:, k, b, :], xln[:, k % XLN, b, :]).then_inc(stats2_done, 1)
                dve.wait_ge(stats2_done, 2 * k + 2)
                nc.vector.bn_aggr(mv2[:, k, 0, :], stats2[:, k, 0, :])
                nc.vector.bn_aggr(mv2[:, k, 1, :], stats2[:, k, 1, :]).then_inc(mv2_done, 1)

            def lo_half(k):
                if k + 1 < NB:
                    dve.wait_ge(hi_done, k + 1)
                    nc.vector.scalar_tensor_tensor(
                        out=mat[:, k, 1, (k + 1) * P:N], in0=mat[:, k, 0, (k + 1) * P:N], scalar=LO_UP,
                        in1=row_part(k, k + 1, NB - 1 - k), op0=ALU.mult, op1=ALU.add).then_inc(lo_done, 1)

            def finish(k):
                d = diag[:, k % DIAG, :]
                dve.wait_ge(gain2_done, k + 1)
                for b in range(2):
                    nc.vector.tensor_scalar(norm2[:, b, :], xln[:, k % XLN, b, :], mv2[:, k, b, 0:1],
                                            gain2[:, k, b:b + 1], ALU.subtract, ALU.mult).then_inc(norm2_done, 1)
                dve.wait_ge(diag_copied, k + 1)
                nc.vector.scalar_tensor_tensor(out=d, in0=ident[:, :], scalar=pre3[:, k, 2:3], in1=d,
                                               op0=ALU.mult, op1=ALU.subtract).then_inc(diag_done, 1)
                dve.wait_ge(ghi2_done, k + 1)
                nc.vector.scalar_tensor_tensor(out=g[:, :, k, 1, :], in0=norm2[:, :, :], scalar=0.0,
                                               in1=g[:, :, k, 0, :], op0=ALU.max, op1=ALU.subtract
                                               ).then_inc(glo2_done, 1)
                dve.wait_ge(diag_hi_done, k + 1)
                nc.vector.scalar_tensor_tensor(
                    out=mat[:, k, 1, k * P:(k + 1) * P], in0=mat[:, k, 0, k * P:(k + 1) * P], scalar=LO_UP,
                    in1=d, op0=ALU.mult, op1=ALU.subtract).then_inc(shell_done, 1)

            dve.wait_ge(ident_done, 1)
            nc.vector.tensor_copy(ident16[:, :], ident[:, :]).then_inc(ident16_done, 1)
            statistics2(0)
            sums(0)
            sums(1)
            lo_half(0)
            finish(0)
            lo_half(1)
            sums(2)
            for k in range(NB - 1):
                statistics2(k + 1)
                if k + 3 < NB:
                    sums(k + 3, 0, 2)
                finish(k + 1)
                if k + 3 < NB:
                    sums(k + 3, 2)
                if k + 2 < NB:
                    lo_half(k + 2)

            def layernorm(b, b_index, par):
                dve.wait_ge(x_here[par], 32 * (b_index + 1))
                for t in range(NB):
                    i = nc.vector.bn_stats(stats[:, t, :], xs[:, par, t, :])
                i.then_inc(stats_done, 1)
                dve.wait_ge(stats_done, b - 1)
                nc.vector.nop(nofuse=True)
                for t in range(NB):
                    i = nc.vector.bn_aggr(mv[:, t, :], stats[:, t, :])
                i.then_inc(mv_done, 1)
                dve.wait_ge(gain_done, b - 1)
                for h in range(2):
                    for t in range(HALF):
                        tt = h * HALF + t
                        i = nc.vector.tensor_scalar(norm[:, tt, :], xs[:, par, tt, :], mv[:, tt, 0:1],
                                                    gain[:, tt:tt + 1], ALU.subtract, ALU.mult)
                    i.then_inc(norm_done, 1)
                    dve.wait_ge(ghi_done, 2 * (b - 2) + h + 1)
                    ts = slice(h * HALF, (h + 1) * HALF)
                    nc.vector.scalar_tensor_tensor(out=g[:, par, ts, 1, :], in0=norm[:, ts, :], scalar=0.0,
                                                   in1=g[:, par, ts, 0, :], op0=ALU.max, op1=ALU.subtract
                                                   ).then_inc(glo_done, 1)

            with dve.Fori(0, B // 2 - 1) as i:
                layernorm(2 * i + 2, i + 1, 0)
                layernorm(2 * i + 3, i + 1, 1)

        @block.scalar
        def _(act):
            def relu(k):
                act.wait_ge(sum_done, t_before[k + 1])
                r = row_part(k, k, NB - k)
                nc.scalar.activation(r, r, ACT.Relu, scale=0.5 * LO_UP, accum_out=rowacc[:, k:k + 1]
                                     ).then_inc(relu_done, 1)

            def hi_half(k):
                if k + 1 < NB:
                    act.wait_ge(relu_done, k + 1)
                    nc.scalar.activation(mat[:, k, 0, (k + 1) * P:N], row_part(k, k + 1, NB - 1 - k), ACT.Copy,
                                         scale=-1.0 / LO_UP).then_inc(hi_done, 1)

            def mirror(k, i):
                if i < len(blocks_of(k + 1)):
                    j, n = blocks_of(k + 1)[i]
                    act.wait_ge(matT_ready, f_before[k] + i + 1)
                    nc.scalar.activation(mat[:, j:j + n, :, k * P:(k + 1) * P], ft[:, 0:n], ACT.Copy
                                         ).then_inc(matT_stored, 1)

            def degree(k):
                act.wait_ge(relu_done, k + 1)
                if k == 0:
                    nc.scalar.activation(deg[:, 0:1], rowacc[:, 0:1], ACT.Copy).then_inc(deg_done, 1)
                else:
                    act.wait_ge(colsum_done, k)
                    nc.scalar.activation(deg[:, k:k + 1], dps[:, k:k + 1], ACT.Identity, bias=rowacc[:, k:k + 1]
                                         ).then_inc(deg_done, 1)

            def finish(k):
                act.wait_ge(norm2_done, 2 * k + 2)
                nc.scalar.activation(g[:, :, k, 0, :], norm2[:, :, :], ACT.Relu).then_inc(ghi2_done, 1)
                act.wait_ge(diag_done, k + 1)
                nc.scalar.activation(mat[:, k, 0, k * P:(k + 1) * P], diag[:, k % DIAG, :], ACT.Copy,
                                     scale=1.0 / LO_UP).then_inc(diag_hi_done, 1)

            relu(0)
            degree(0)
            hi_half(0)
            finish(0)
            relu(1)
            hi_half(1)
            for k in range(NB):
                if k + 1 < NB:
                    degree(k + 1)
                if k + 2 < NB:
                    relu(k + 2)
                mirror(k, 0)
                if k + 2 < NB:
                    hi_half(k + 2)
                mirror(k, 1)
                if k + 1 < NB:
                    finish(k + 1)
                mirror(k, 2)
                mirror(k, 3)

            def u_copy(c, j):
                act.wait_ge(acc_ready, c + 1)
                nc.scalar.activation(u_sb[:, j % 2], acc[:, j, :], ACT.Copy).then_inc(u_ready, 1)

            def relu_out(c, j, first_users):
                act.wait_ge(uw_ready, c + 1)
                if first_users is not None:
                    act.wait_ge(stored[j % 2], 16 * first_users)
                for t in range(BPC):
                    i = nc.scalar.activation(o_sb[:, j % 2, t, :], tp[:, j % 2, t * P:(t + 1) * P], ACT.Relu,
                                             scale=y_out[:, j * BPC + t:j * BPC + t + 1])
                i.then_inc(relu_out_done, 1)

            act.wait_ge(y_done, 2)
            u_copy(0, 0)
            u_copy(1, 1)
            for j in range(2, NCH):
                act.wait_ge(uw_ready, j - 1)
                u_copy(j, j)
                relu_out(j - 2, j - 2, None)
            relu_out(NCH - 2, NCH - 2, 1)

            def g_hi(b, h, par):
                act.wait_ge(norm_done, 2 * (b - 2) + h + 1)
                ts = slice(h * HALF, (h + 1) * HALF)
                if h == 0:
                    act.wait_ge(acc_ready, NCH * (b - 1))
                nc.scalar.activation(g[:, par, ts, 0, :], norm[:, ts, :], ACT.Relu).then_inc(ghi_done, 1)

            def batch(b, par, ln):
                for j in range(NCH):
                    if ln and j >= NCH - 2:
                        g_hi(b + 1, j - (NCH - 2), 1 - par)
                    c = NCH * b + j
                    act.wait_ge(uw_ready, c - 1)
                    u_copy(c, j)
                    relu_out(c - 1, (j - 1) % NCH, 2 * b + (j - 1) // 2)

            with act.Fori(0, B // 2 - 1) as i:
                batch(2 * i + 1, 1, True)
                batch(2 * i + 2, 0, True)
            batch(B - 1, 1, False)
            relu_out(NCH * B - 1, NCH - 1, (NCH * B - 1) // 2)

        @block.tensor
        def _(pe):
            def adj_transposes(k, i, j, n):
                c = t_before[k] + i
                if k == 0:
                    pe.wait_ge(piece_here[i], 32)
                elif i == 0:
                    pe.wait_ge(row_here[k % ROWS], 16 * row_loads(k))
                    if k + 1 < NB:
                        pe.wait_ge(col_here[k % COLS], 16 * col_loads(k))
                if c >= 2:
                    pe.wait_ge(sum_done, c - 1)
                for b in range(n):
                    src = row_part(k, k, 1) if j + b == k else col_part(k, j + b)
                    t = nc.tensor.transpose(tp[:, c % 2, b * P:(b + 1) * P], src, ident[:, :])
                t.then_inc(adjT_ready, 1)

            def mat_transposes(k, i, j, n):
                c = f_before[k] + i
                if c >= 1:
                    pe.wait_ge(matT_stored, c)
                for b in range(n):
                    for h in range(2):
                        t = nc.tensor.transpose(ft[:, b, h, :], mat[:, k, h, (j + b) * P:(j + b + 1) * P],
                                                ident16[:, :])
                t.then_inc(matT_ready, 1)

            def column_sums(k):
                pe.wait_ge(lo_done, k + 1)
                if k >= 1:
                    pe.wait_ge(deg_done, k + 1)
                for j in range(k + 1, NB):
                    for h, ones in ((0, ones_hi), (1, ones_lo)):
                        m = nc.tensor.matmul(dps[:, j:j + 1], mat[:, k, h, j * P:(j + 1) * P], ones[:, :],
                                             start=(k == 0 and j == 1 and h == 0), stop=False,
                                             skip_group_check=True)
                m.then_inc(colsum_done, 1)

            def products(m, j, par):
                cols = slice(j * CW, (j + 1) * CW)
                nc.tensor.matmul(acc[:, j, :], g[:, par, m, 0, :], mat[:, m, 0, cols], start=(m == 0), stop=False)
                nc.tensor.matmul(acc[:, j, :], g[:, par, m, 1, :], mat[:, m, 0, cols], start=False, stop=False)
                return nc.tensor.matmul(acc[:, j, :], g[:, par, m, 2, :], mat[:, m, 1, cols],
                                        start=False, stop=(m == NB - 1))

            def times_w(c, j, ordinary):
                pe.wait_ge(u_ready, c + 1)
                if ordinary:
                    pe.wait_ge(relu_out_done, c - 1)
                for t in range(BPC):
                    i = nc.tensor.matmul(tp[:, j % 2, t * P:(t + 1) * P], u_sb[:, j % 2, t * P:(t + 1) * P],
                                         w_sb[:, :], start=True, stop=True)
                i.then_inc(uw_ready, 1)

            pe.wait_ge(ident_done, 1)
            pe.wait_ge(ident16_done, 1)
            pe.wait_ge(consts_done, 2)
            for k in range(3):
                for i, (j, n) in enumerate(blocks_of(k)):
                    adj_transposes(k, i, j, n)
                if k == 1:
                    column_sums(0)
            for k in range(NB):
                if k >= 1:
                    pe.wait_ge(matT_stored, f_before[k])
                pe.wait_ge(glo2_done, k + 1)
                pe.wait_ge(gneg2_done, k + 1)
                pe.wait_ge(shell_done, k + 1)
                ahead = blocks_of(k + 3) if k + 3 < NB else []
                mirror = blocks_of(k + 1)
                for j in range(NCH):
                    last = products(k, j, 0)
                    if k == NB - 1:
                        last.then_inc(acc_ready, 1)
                        if j == 1:
                            pe.wait_ge(w_here, 16)
                        if j >= 1:
                            times_w(j - 1, j - 1, j - 1 >= 2)
                    if j < len(ahead):
                        adj_transposes(k + 3, j, *ahead[j])
                    if j < len(mirror):
                        mat_transposes(k, j, *mirror[j])
                if k + 2 < NB:
                    column_sums(k + 1)

            def batch(b, par, waits_for_g=True):
                for j in range(NCH):
                    c = NCH * b + j
                    pe.wait_ge(u_ready, c - NCH + 1)
                    for m in range(NB):
                        if waits_for_g and j == 0 and m % HALF == 0:
                            pe.wait_ge(glo_done, 2 * (b - 2) + m // HALF + 1)
                            pe.wait_ge(gneg_done, 2 * (b - 2) + m // HALF + 1)
                        last = products(m, j, par)
                    last.then_inc(acc_ready, 1)
                    times_w(c - 1, (j - 1) % NCH, True)

            batch(1, 1, waits_for_g=False)
            with pe.Fori(1, B // 2) as i:
                batch(2 * i, 0)
                batch(2 * i + 1, 1)
            times_w(NCH * B - 1, NCH - 1, True)


_INS = ['x', 'adj', 'L0_gnn_W']
_OUTS = [((8, 2048, 128), 'float32')]


def kernel(**inputs):
    import numpy as _np
    import concourse.bacc as _bacc
    from concourse import mybir as _mybir
    from concourse.bass_utils import run_bass_kernel_spmd as _run

    nc = _bacc.Bacc("TRN2", target_bir_lowering=False, num_devices=1)
    arrays, args = {}, []
    for name in _INS:
        a = _np.ascontiguousarray(inputs[name])
        arrays[f"in_{name}_dram"] = a
        args.append(nc.dram_tensor(f"in_{name}_dram", a.shape, _mybir.dt.from_np(a.dtype), kind="ExternalInput").ap())
    for i, (shape, dtype) in enumerate(_OUTS):
        dt = _mybir.dt.from_np(_np.dtype(dtype))
        args.append(nc.dram_tensor(f"out_{i}_dram", shape, dt, kind="ExternalOutput").ap())
    gnn_kernel(nc, *args)
    r = _run(nc, [arrays], core_ids=[0])
    got = tuple(r.results[0][f"out_{i}_dram"] for i in range(len(_OUTS)))
    return got[0]
```

```python
from contextlib import ExitStack

import concourse.bass as bass
from concourse import mybir

ALU = mybir.AluOpType
ACT = mybir.ActivationFunctionType
F32 = mybir.dt.float32
F16 = mybir.dt.float16

P = 128
LN_EPS = 1e-5
LO_UP = 2048.0
G_UP = 2048.0
U_DOWN = 8.0
W_UP = 1024.0


def gnn_kernel(nc: bass.Bass, x: bass.AP, adj: bass.AP, W: bass.AP, out: bass.AP):
    B, N, F = x.shape
    NB = N // P
    CW = 512
    BPC = CW // P
    NCH = N // CW
    ROWS, COLS, XLN, DIAG = 4, 2, 4, 3
    HALF = NB // 2
    HCW = CW // 2
    LAST = B * NCH - 1
    assert F == P and B % 2 == 0 and NB % BPC == 0

    row_at, col_at, at = [], [], 0
    for s in range(ROWS):
        row_at.append(at)
        at += (NB - s) * P
    for s in range(COLS):
        col_at.append(at)
        at += (NB - 1 - s) * P
    STAGE = at

    def blocks_of(first):
        return [(j, min(BPC, NB - j)) for j in range(first, NB, BPC)]

    t_before = [sum(len(blocks_of(s)) for s in range(k)) for k in range(NB + 1)]
    f_before = [sum(len(blocks_of(s + 1)) for s in range(k)) for k in range(NB + 1)]

    with ExitStack() as ctx:
        def sb(name, shape, dt):
            return ctx.enter_context(nc.sbuf_tensor(name, shape, dt))

        def psum(name, shape, dt):
            return ctx.enter_context(nc.psum_tensor(name, shape, dt))

        def sem(name):
            return ctx.enter_context(nc.semaphore(name))

        mat = sb("mat", [P, NB, 2, N], F16)
        stage = sb("stage", [P, STAGE], F32)
        xln = sb("xln", [P, XLN, 2, F], F32)
        g = sb("g", [P, 2, NB, 3, F], F16)
        diag = sb("diag", [P, DIAG, P], F32)
        norm2 = sb("norm2", [P, 2, F], F32)
        w_sb = sb("w_sb", [F, F], F32)
        w16 = sb("w16", [F, 3, F], F16)
        ident = sb("ident", [P, P], F32)
        ident16 = sb("ident16", [P, P], F16)
        ones_hi = sb("ones_hi", [P, 1], F16)
        ones_lo = sb("ones_lo", [P, 1], F16)
        minus_half = sb("minus_half", [P, NB], F32)
        colacc = sb("colacc", [P, NB], F32)
        rowacc = sb("rowacc", [P, NB], F32)
        deg = sb("deg", [P, NB], F32)
        stats2 = sb("stats2", [P, NB, 2, 6], F32)
        mv2 = sb("mv2", [P, NB, 2, 2], F32)
        pre3 = sb("pre3", [P, NB, 3], F32)
        inv3 = sb("inv3", [P, NB, 3], F32)
        gain2 = sb("gain2", [P, NB, 2], F32)
        y_in = sb("y_in", [P, NB], F32)
        y_out = sb("y_out", [P, NB], F32)
        stats = sb("stats", [P, NB, 6], F32)
        mv = sb("mv", [P, NB, 2], F32)
        veps = sb("veps", [P, NB], F32)
        rstd = sb("rstd", [P, NB], F32)
        gain = sb("gain", [P, NB], F32)

        xs = stage[:, 0:2 * NB * F].rearrange("p (b t f) -> p b t f", b=2, t=NB)
        at = 2 * NB * F
        norm = stage[:, at:at + NB * F].rearrange("p (t f) -> p t f", t=NB)
        at += NB * F
        u16 = stage[:, at:at + 2 * CW].bitcast(F16).rearrange("p (s h n) -> p s h n", s=2, h=2)
        at += 2 * CW
        o_sb = stage[:, at:at + 2 * CW].rearrange("p (s t f) -> p s t f", s=2, f=F)

        acc = psum("acc", [P, NCH, CW], F32)
        tp = psum("tp", [P, 2, CW], F32)
        ft = psum("ft", [P, 2, BPC, 2, P], F16)

        ident_zero = sem("ident_zero")
        ident_done = sem("ident_done")
        ident16_done = sem("ident16_done")
        consts_done = sem("consts_done")
        w_here = sem("w_here")
        row_here = [sem(f"row_here{s}") for s in range(ROWS)]
        col_here = [sem(f"col_here{s}") for s in range(COLS)]
        xln_here = [sem(f"xln_here{s}") for s in range(XLN)]
        piece_here = [sem(f"piece_here{i}") for i in range(NCH)]
        adjT_ready = sem("adjT_ready")
        sum_done = sem("sum_done")
        relu_done = sem("relu_done")
        hi_done = sem("hi_done")
        lo_done = sem("lo_done")
        colsum_ready = sem("colsum_ready")
        colacc_done = sem("colacc_done")
        deg_done = sem("deg_done")
        pre3_done = sem("pre3_done")
        inv3_done = sem("inv3_done")
        diag_copied = sem("diag_copied")
        diag_done = sem("diag_done")
        diag_hi_done = sem("diag_hi_done")
        shell_done = sem("shell_done")
        matT_ready = sem("matT_ready")
        matT_stored = sem("matT_stored")
        stats2_done = sem("stats2_done")
        mv2_done = sem("mv2_done")
        gain2_done = sem("gain2_done")
        norm2_done = sem("norm2_done")
        ghi2_done = sem("ghi2_done")
        glo2_done = sem("glo2_done")
        gneg2_done = sem("gneg2_done")
        y_done = sem("y_done")
        w_hi_done = sem("w_hi_done")
        w_neg_done = sem("w_neg_done")
        w_lo_done = sem("w_lo_done")
        acc_ready = sem("acc_ready")
        u_hi_done = sem("u_hi_done")
        u_lo_done = sem("u_lo_done")
        uw_ready = sem("uw_ready")
        relu_out_done = sem("relu_out_done")
        add_done = sem("add_done")
        last_relu_done = sem("last_relu_done")
        last_add_done = sem("last_add_done")
        stored = [sem(f"stored{s}") for s in range(2)]
        x_here = [sem(f"x_here{s}") for s in range(2)]
        stats_done = sem("stats_done")
        mv_done = sem("mv_done")
        veps_done = sem("veps_done")
        rstd_done = sem("rstd_done")
        gain_done = sem("gain_done")
        norm_done = sem("norm_done")
        ghi_done = sem("ghi_done")
        glo_done = sem("glo_done")
        gneg_done = sem("gneg_done")

        x_blocks = x.rearrange("b (t p) f -> b p t f", p=P)
        out_blocks = out.rearrange("b (t p) f -> b p t f", p=P)

        def row_part(k, j, n):
            o = row_at[k % ROWS] + (j - k) * P
            return stage[:, o:o + n * P]

        def col_part(k, j):
            o = col_at[k % COLS] + (j - k - 1) * P
            return stage[:, o:o + P]

        def row_loads(k):
            return k // ROWS + (k % ROWS != 0)

        def col_loads(k):
            return k // COLS + (k % COLS != 0)

        PRODUCTS = [0, 0, 4, 4, 4, 4, 4, 3, 4, 3, 4, 3, 4, 3, 4, 3, 4, 5, 4]
        steps, products_done = [], 0
        for s in range(len(PRODUCTS)):
            step = [("C", s - 2, 0)] if 0 <= s - 2 < NB - 1 else []
            for i in range(NCH):
                if s < NB and i < len(blocks_of(s)):
                    step.append(("T", s, i))
                if 0 <= s - 2 < NB - 1 and i < len(blocks_of(s - 1)):
                    step.append(("M", s - 2, i))
            due = [("P", p // NCH, p % NCH) for p in range(products_done, products_done + PRODUCTS[s])]
            products_done += PRODUCTS[s]
            steps.append(step[:-1] + due[:1] + step[-1:] + due[1:])
        assert products_done == NB * NCH
        uses = [u for step in steps for u in step if u[0] in "TC"]
        use_of = {u: n for n, u in enumerate(uses)}

        def tp_free(pe, n):
            if n >= 2:
                kind, k, i = uses[n - 2]
                if kind == "T":
                    pe.wait_ge(sum_done, t_before[k] + i + 1)
                else:
                    pe.wait_ge(colacc_done, k + 1)

        block = ctx.enter_context(nc.Block())

        @block.sync
        def _(sp):
            def load_shell(k):
                if k >= ROWS:
                    sp.wait_ge(lo_done, k - ROWS + 1)
                    sp.wait_ge(diag_copied, k - ROWS + 1)
                sp.dma_start(row_part(k, k, NB - k), adj[k * P:(k + 1) * P, k * P:N]).then_inc(row_here[k % ROWS], 16)
                if k + 1 < NB:
                    if k >= COLS:
                        sp.wait_ge(adjT_ready, t_before[k - COLS + 1])
                    dst = stage[:, col_at[k % COLS]:col_at[k % COLS] + (NB - 1 - k) * P]
                    sp.dma_start(dst.rearrange("p (j c) -> p j c", c=P),
                                 adj[(k + 1) * P:N, k * P:(k + 1) * P].rearrange("(j p) c -> p j c", p=P)
                                 ).then_inc(col_here[k % COLS], 16)
                load_xln(k)

            def load_xln(k):
                if k >= XLN:
                    sp.wait_ge(norm2_done, 2 * (k - XLN + 1))
                sp.dma_start(xln[:, k % XLN], x[0:2, k * P:(k + 1) * P, :].rearrange("b p f -> p b f")
                             ).then_inc(xln_here[k % XLN], 16)

            for i, (j, n) in enumerate(blocks_of(0)):
                sp.dma_start(row_part(0, j, n), adj[0:P, j * P:(j + n) * P]).then_inc(piece_here[i], 16)
                jc, nc_ = (1, n - 1) if j == 0 else (j, n)
                dst = stage[:, col_at[0] + (jc - 1) * P:col_at[0] + (jc - 1 + nc_) * P]
                sp.dma_start(dst.rearrange("p (j c) -> p j c", c=P),
                             adj[jc * P:(jc + nc_) * P, 0:P].rearrange("(j p) c -> p j c", p=P)
                             ).then_inc(piece_here[i], 16)
                if i == 0:
                    load_xln(0)
            for k in range(1, NB):
                load_shell(k)
                if k == 1:
                    sp.dma_start(w_sb[:, :], W).then_inc(w_here, 16)

            def load_x(b, par):
                for h in range(2):
                    ts = slice(h * HALF, (h + 1) * HALF)
                    sp.dma_start(xs[:, par, ts, :], x_blocks[b, :, ts, :]).then_inc(x_here[par], 16)

            sp.wait_ge(shell_done, NB)
            load_x(0, 0)
            load_x(1, 1)

            def store(b, j, par):
                sp.wait_ge(add_done, NCH * b + j + 1)
                sp.dma_start(out_blocks[b, :, j * BPC:(j + 1) * BPC, :], o_sb[:, par]).then_inc(stored[par], 16)

            for j in range(NCH):
                store(0, j, j % 2)

            with sp.Fori(0, B // 2 - 1) as i:
                for b, par in ((2 * i + 1, 1), (2 * i + 2, 0)):
                    sp.wait_ge(add_done, NCH * b)
                    load_x(b + 1, 1 - par)
                    for j in range(NCH):
                        store(b, j, j % 2)
            for j in range(NCH - 1):
                store(B - 1, j, j % 2)
            for h in range(2):
                sp.wait_ge(last_add_done, h + 1)
                t = (NCH - 1) * BPC + 2 * h
                sp.dma_start(out_blocks[B - 1, :, t:t + 2, :], o_sb[:, 1, 2 * h:2 * h + 2]).then_inc(stored[1], 16)
            sp.wait_ge(stored[0], 16 * B * NCH // 2)
            sp.wait_ge(stored[1], 16 * (B * NCH // 2 + 1))

        @block.gpsimd
        def _(pool):
            nc.gpsimd.memset(ident[:, :], 0.0).then_inc(ident_zero, 1)
            pool.wait_ge(ident_zero, 1)
            nc.gpsimd.affine_select(out=ident[:, :], in_=ident[:, :], compare_op=ALU.not_equal, fill=1.0,
                                    base=0, pattern=[[-1, P]], channel_multiplier=1).then_inc(ident_done, 1)
            nc.gpsimd.memset(ones_hi[:, :], -LO_UP).then_inc(consts_done, 1)
            nc.gpsimd.memset(ones_lo[:, :], 1.0).then_inc(consts_done, 1)
            nc.gpsimd.memset(minus_half[:, :], -0.5).then_inc(consts_done, 1)
            nc.gpsimd.memset(colacc[:, 1:NB], 0.0).then_inc(consts_done, 1)
            pool.wait_ge(consts_done, 4)

            def copy_diag(k):
                pool.wait_ge(relu_done, k + 1)
                if k >= DIAG:
                    pool.wait_ge(shell_done, k - DIAG + 1)
                nc.gpsimd.tensor_scalar(diag[:, k % DIAG, :], row_part(k, k, 1), 1.0, 1.0, ALU.mult, ALU.mult
                                        ).then_inc(diag_copied, 1)

            def hi_half(k):
                if k + 1 < NB:
                    pool.wait_ge(relu_done, k + 1)
                    nc.gpsimd.tensor_scalar(mat[:, k, 0, (k + 1) * P:N], row_part(k, k + 1, NB - 1 - k),
                                            -1.0 / LO_UP, 1.0, ALU.mult, ALU.mult).then_inc(hi_done, 1)

            def factors(k):
                pool.wait_ge(relu_done, k + 1)
                if k >= 1:
                    pool.wait_ge(colacc_done, k)
                nc.gpsimd.tensor_tensor(deg[:, k:k + 1], rowacc[:, k:k + 1], colacc[:, k:k + 1], ALU.add
                                        ).then_inc(deg_done, 1)
                pool.wait_ge(deg_done, k + 1)
                nc.gpsimd.tensor_scalar(pre3[:, k, 2:3], deg[:, k:k + 1], 0.0, deg[:, k:k + 1], ALU.is_le, ALU.add
                                        ).then_inc(pre3_done, 1)
                pool.wait_ge(pre3_done, 2 * k + 2)
                nc.gpsimd.tensor_tensor(inv3[:, k, :], pre3[:, k, :], minus_half[:, 0:3], ALU.pow
                                        ).then_inc(inv3_done, 1)
                pool.wait_ge(inv3_done, k + 1)
                nc.gpsimd.tensor_scalar(gain2[:, k, :], inv3[:, k, 0:2], inv3[:, k, 2:3], G_UP, ALU.mult, ALU.mult
                                        ).then_inc(gain2_done, 1)

            def variances(k):
                pool.wait_ge(mv2_done, k + 1)
                nc.gpsimd.tensor_scalar(pre3[:, k, 0:2], mv2[:, k, :, 1], LN_EPS, None, ALU.add
                                        ).then_inc(pre3_done, 1)

            for s in range(NB + 1):
                if s >= 1:
                    factors(s - 1)
                    copy_diag(s - 1)
                if s < NB:
                    variances(s)
                    if s >= 1:
                        hi_half(s)
            nc.gpsimd.tensor_scalar(y_in[:, :], inv3[:, :, 2], G_UP, 1.0, ALU.mult, ALU.mult).then_inc(y_done, 1)
            nc.gpsimd.tensor_scalar(y_out[:, :], inv3[:, :, 2], LO_UP / G_UP * U_DOWN / W_UP, 1.0, ALU.mult, ALU.mult
                                    ).then_inc(y_done, 1)
            pool.wait_ge(y_done, 2)

            def add_x(b, j, par):
                pool.wait_ge(relu_out_done, NCH * b + j + 1)
                o = o_sb[:, j % 2]
                nc.gpsimd.tensor_tensor(o, o, xs[:, par, j * BPC:(j + 1) * BPC, :], ALU.add).then_inc(add_done, 1)

            def gains(b):
                pool.wait_ge(mv_done, b - 1)
                nc.gpsimd.nop(nofuse=True)
                nc.gpsimd.tensor_scalar(veps[:, :], mv[:, :, 1], LN_EPS, None, ALU.add).then_inc(veps_done, 1)
                pool.wait_ge(veps_done, b - 1)
                nc.gpsimd.tensor_tensor(rstd[:, :], veps[:, :], minus_half[:, :], ALU.pow).then_inc(rstd_done, 1)
                pool.wait_ge(rstd_done, b - 1)
                nc.gpsimd.tensor_tensor(gain[:, :], rstd[:, :], y_in[:, :], ALU.mult).then_inc(gain_done, 1)

            def g_neg(b, h, par):
                pool.wait_ge(glo_done, 2 * (b - 2) + h + 1)
                nc.gpsimd.nop(nofuse=True)
                t = slice(h * HALF, (h + 1) * HALF)
                nc.gpsimd.tensor_scalar(g[:, par, t, 2, :], g[:, par, t, 0, :], -1.0 / LO_UP, 1.0,
                                        ALU.mult, ALU.mult).then_inc(gneg_done, 1)

            pool.wait_ge(x_here[0], 32)
            for j in range(NCH - 1):
                add_x(0, j, 0)

            with pool.Fori(0, B // 2 - 1) as i:
                for b, par in ((2 * i + 1, 1), (2 * i + 2, 0)):
                    add_x(b - 1, NCH - 1, 1 - par)
                    gains(b + 1)
                    pool.wait_ge(x_here[par], 32 * (i + 2 - par))
                    add_x(b, 0, par)
                    g_neg(b + 1, 0, 1 - par)
                    add_x(b, 1, par)
                    g_neg(b + 1, 1, 1 - par)
                    add_x(b, 2, par)
            add_x(B - 2, NCH - 1, 0)
            for j in range(NCH - 1):
                add_x(B - 1, j, 1)

        @block.vector
        def _(dve):
            def sums(k, first=0, last=NCH):
                for i, (j, n) in list(enumerate(blocks_of(k)))[first:last]:
                    c = t_before[k] + i
                    if k == 0:
                        dve.wait_ge(piece_here[i], 32)
                    elif i == 0:
                        dve.wait_ge(row_here[k % ROWS], 16 * row_loads(k))
                    dve.wait_ge(adjT_ready, c + 1)
                    bank = use_of["T", k, i] % 2
                    nc.vector.tensor_tensor(row_part(k, j, n), row_part(k, j, n), tp[:, bank, 0:n * P], ALU.add
                                            ).then_inc(sum_done, 1)

            def add_colsums(k):
                if k == 0:
                    dve.wait_ge(consts_done, 4)
                dve.wait_ge(colsum_ready, k + 1)
                c = colacc[:, k + 1:NB]
                nc.vector.tensor_tensor(c, c, tp[:, use_of["C", k, 0] % 2, k + 1:NB], ALU.add).then_inc(colacc_done, 1)

            def statistics2(k):
                dve.wait_ge(xln_here[k % XLN], 16 * (k // XLN + 1))
                for b in range(2):
                    nc.vector.bn_stats(stats2[:, k, b, :], xln[:, k % XLN, b, :]).then_inc(stats2_done, 1)
                dve.wait_ge(stats2_done, 2 * k + 2)
                nc.vector.bn_aggr(mv2[:, k, 0, :], stats2[:, k, 0, :])
                nc.vector.bn_aggr(mv2[:, k, 1, :], stats2[:, k, 1, :]).then_inc(mv2_done, 1)

            def lo_half(k):
                if k + 1 < NB:
                    dve.wait_ge(hi_done, k + 1)
                    nc.vector.scalar_tensor_tensor(
                        out=mat[:, k, 1, (k + 1) * P:N], in0=mat[:, k, 0, (k + 1) * P:N], scalar=LO_UP,
                        in1=row_part(k, k + 1, NB - 1 - k), op0=ALU.mult, op1=ALU.add).then_inc(lo_done, 1)

            def diagonal(k):
                d = diag[:, k % DIAG, :]
                dve.wait_ge(pre3_done, 2 * k + 2)
                dve.wait_ge(diag_copied, k + 1)
                nc.vector.scalar_tensor_tensor(out=d, in0=ident[:, :], scalar=pre3[:, k, 2:3], in1=d,
                                               op0=ALU.mult, op1=ALU.subtract).then_inc(diag_done, 1)

            def normalize2(k):
                dve.wait_ge(gain2_done, k + 1)
                if k >= 1:
                    dve.wait_ge(glo2_done, k)
                for b in range(2):
                    nc.vector.tensor_scalar(norm2[:, b, :], xln[:, k % XLN, b, :], mv2[:, k, b, 0:1],
                                            gain2[:, k, b:b + 1], ALU.subtract, ALU.mult).then_inc(norm2_done, 1)

            def g_lo2(k):
                dve.wait_ge(ghi2_done, k + 1)
                nc.vector.scalar_tensor_tensor(out=g[:, :, k, 1, :], in0=norm2[:, :, :], scalar=0.0,
                                               in1=g[:, :, k, 0, :], op0=ALU.max, op1=ALU.subtract
                                               ).then_inc(glo2_done, 1)

            def diagonal_lo(k):
                dve.wait_ge(diag_hi_done, k + 1)
                nc.vector.scalar_tensor_tensor(
                    out=mat[:, k, 1, k * P:(k + 1) * P], in0=mat[:, k, 0, k * P:(k + 1) * P], scalar=LO_UP,
                    in1=diag[:, k % DIAG, :], op0=ALU.mult, op1=ALU.subtract).then_inc(shell_done, 1)

            dve.wait_ge(ident_done, 1)
            nc.vector.tensor_copy(ident16[:, :], ident[:, :]).then_inc(ident16_done, 1)
            for s in range(NB + 2):
                if s >= 2:
                    normalize2(s - 2)
                    if s - 2 < NB - 1:
                        add_colsums(s - 2)
                    diagonal_lo(s - 2)
                if s < NB:
                    sums(s, 0, 1)
                if s >= 2:
                    g_lo2(s - 2)
                if s < NB:
                    sums(s, 1)
                if 1 <= s <= NB:
                    lo_half(s - 1)
                if s < NB:
                    statistics2(s)
                if 1 <= s <= NB:
                    diagonal(s - 1)
                if s == NB - 1:
                    dve.wait_ge(w_hi_done, 1)
                    nc.vector.scalar_tensor_tensor(out=w16[:, 1], in0=w_sb[:, :], scalar=W_UP, in1=w16[:, 0],
                                                   op0=ALU.mult, op1=ALU.subtract).then_inc(w_lo_done, 1)

            def u_lo(c, j):
                dve.wait_ge(u_hi_done, c + 1)
                nc.vector.scalar_tensor_tensor(out=u16[:, j % 2, 1], in0=u16[:, j % 2, 0], scalar=U_DOWN,
                                               in1=acc[:, j, :], op0=ALU.mult, op1=ALU.subtract
                                               ).then_inc(u_lo_done, 1)

            def statistics(b, b_index, par):
                dve.wait_ge(x_here[par], 32 * (b_index + 1))
                for t in range(NB):
                    i = nc.vector.bn_stats(stats[:, t, :], xs[:, par, t, :])
                i.then_inc(stats_done, 1)
                dve.wait_ge(stats_done, b - 1)
                nc.vector.nop(nofuse=True)
                for t in range(NB):
                    i = nc.vector.bn_aggr(mv[:, t, :], stats[:, t, :])
                i.then_inc(mv_done, 1)

            def normalize(b, h, par):
                dve.wait_ge(gain_done, b - 1)
                for t in range(h * HALF, (h + 1) * HALF):
                    i = nc.vector.tensor_scalar(norm[:, t, :], xs[:, par, t, :], mv[:, t, 0:1],
                                                gain[:, t:t + 1], ALU.subtract, ALU.mult)
                i.then_inc(norm_done, 1)

            def g_lo(b, h, par):
                dve.wait_ge(ghi_done, 2 * (b - 2) + h + 1)
                ts = slice(h * HALF, (h + 1) * HALF)
                nc.vector.scalar_tensor_tensor(out=g[:, par, ts, 1, :], in0=norm[:, ts, :], scalar=0.0,
                                               in1=g[:, par, ts, 0, :], op0=ALU.max, op1=ALU.subtract
                                               ).then_inc(glo_done, 1)

            def batch(b, par, b_index):
                c = NCH * b
                u_lo(c, 0)
                u_lo(c + 1, 1)
                statistics(b + 1, b_index, 1 - par)
                normalize(b + 1, 0, 1 - par)
                normalize(b + 1, 1, 1 - par)
                g_lo(b + 1, 0, 1 - par)
                u_lo(c + 2, 2)
                g_lo(b + 1, 1, 1 - par)
                u_lo(c + 3, 3)

            for j in range(NCH):
                u_lo(j, j)
            with dve.Fori(0, B // 2 - 1) as i:
                batch(2 * i + 1, 1, i + 1)
                batch(2 * i + 2, 0, i + 1)
            for j in range(NCH - 1):
                u_lo(NCH * (B - 1) + j, j)
            for h in range(2):
                n = slice(h * HCW, (h + 1) * HCW)
                dve.wait_ge(u_hi_done, LAST + 1 + h)
                nc.vector.scalar_tensor_tensor(out=u16[:, 1, 1, n], in0=u16[:, 1, 0, n], scalar=U_DOWN,
                                               in1=acc[:, (NCH - 1) * (1 - h), 0:HCW],
                                               op0=ALU.mult, op1=ALU.subtract).then_inc(u_lo_done, 1)
                dve.wait_ge(uw_ready, LAST + 2 + 2 * h)
                dve.wait_ge(stored[1], 16 * (LAST // 2))
                k = (NCH - 1) * BPC + 2 * h + 1
                nc.vector.tensor_scalar(o_sb[:, 1, 2 * h + 1, :], acc[:, 1 + h, 0:P], y_out[:, k:k + 1], 0.0,
                                        ALU.mult, ALU.max).then_inc(last_relu_done, 1)
                dve.wait_ge(last_relu_done, h + 1)
                dve.wait_ge(relu_out_done, LAST + 1 + h)
                o = o_sb[:, 1, 2 * h:2 * h + 2]
                t = (NCH - 1) * BPC + 2 * h
                nc.vector.tensor_tensor(o, o, xs[:, 1, t:t + 2, :], ALU.add).then_inc(last_add_done, 1)

        @block.scalar
        def _(act):
            def relu(k):
                if k == 0:
                    for h, total in ((0, rowacc), (1, colacc)):
                        act.wait_ge(sum_done, (h + 1) * NCH // 2)
                        r = row_part(0, h * HALF, HALF)
                        i = nc.scalar.activation(r, r, ACT.Relu, scale=0.5 * LO_UP, accum_out=total[:, 0:1])
                    i.then_inc(relu_done, 1)
                    return
                act.wait_ge(sum_done, t_before[k + 1])
                r = row_part(k, k, NB - k)
                nc.scalar.activation(r, r, ACT.Relu, scale=0.5 * LO_UP, accum_out=rowacc[:, k:k + 1]
                                     ).then_inc(relu_done, 1)

            def mirror(k, i):
                if i < len(blocks_of(k + 1)):
                    j, n = blocks_of(k + 1)[i]
                    c = f_before[k] + i
                    act.wait_ge(matT_ready, c + 1)
                    nc.scalar.activation(mat[:, j:j + n, :, k * P:(k + 1) * P], ft[:, c % 2, 0:n], ACT.Copy
                                         ).then_inc(matT_stored, 1)

            def diagonal_hi(k):
                act.wait_ge(diag_done, k + 1)
                nc.scalar.activation(mat[:, k, 0, k * P:(k + 1) * P], diag[:, k % DIAG, :], ACT.Copy,
                                     scale=1.0 / LO_UP).then_inc(diag_hi_done, 1)

            def g_hi2(k):
                act.wait_ge(norm2_done, 2 * k + 2)
                nc.scalar.activation(g[:, :, k, 0, :], norm2[:, :, :], ACT.Relu).then_inc(ghi2_done, 1)
                act.wait_ge(ghi2_done, k + 1)
                nc.scalar.activation(g[:, :, k, 2, :], g[:, :, k, 0, :], ACT.Copy, scale=-1.0 / LO_UP
                                     ).then_inc(gneg2_done, 1)

            for s in range(NB + 1):
                if s >= 2:
                    mirror(s - 2, 0)
                    mirror(s - 2, 1)
                if s < NB:
                    relu(s)
                if s >= 2:
                    mirror(s - 2, 2)
                    mirror(s - 2, 3)
                if s == 0:
                    act.wait_ge(relu_done, 1)
                    nc.scalar.activation(mat[:, 0, 0, P:N], row_part(0, 1, NB - 1), ACT.Copy, scale=-1.0 / LO_UP
                                         ).then_inc(hi_done, 1)
                if s >= 1:
                    diagonal_hi(s - 1)
                    g_hi2(s - 1)
                if s == NB - 2:
                    act.wait_ge(w_here, 16)
                    nc.scalar.activation(w16[:, 0], w_sb[:, :], ACT.Copy, scale=W_UP).then_inc(w_hi_done, 1)
                    act.wait_ge(w_hi_done, 1)
                    nc.scalar.activation(w16[:, 2], w16[:, 0], ACT.Copy, scale=-1.0 / U_DOWN).then_inc(w_neg_done, 1)

            def u_hi(c, j):
                act.wait_ge(acc_ready, c + 1)
                nc.scalar.activation(u16[:, j % 2, 0], acc[:, j, :], ACT.Copy, scale=1.0 / U_DOWN
                                     ).then_inc(u_hi_done, 1)

            def relu_out(c, j, earlier_stores):
                act.wait_ge(uw_ready, c + 1)
                if earlier_stores is not None:
                    act.wait_ge(stored[j % 2], 16 * earlier_stores)
                for t in range(BPC):
                    i = nc.scalar.activation(o_sb[:, j % 2, t, :], tp[:, j % 2, t * P:(t + 1) * P], ACT.Relu,
                                             scale=y_out[:, j * BPC + t:j * BPC + t + 1])
                i.then_inc(relu_out_done, 1)

            act.wait_ge(y_done, 2)
            act.wait_ge(shell_done, NB)
            u_hi(0, 0)
            u_hi(1, 1)
            for j in range(2, NCH):
                act.wait_ge(uw_ready, j - 1)
                u_hi(j, j)
                relu_out(j - 2, j - 2, None)
            relu_out(NCH - 2, NCH - 2, 1)

            def g_hi(b, h, par):
                act.wait_ge(norm_done, 2 * (b - 2) + h + 1)
                ts = slice(h * HALF, (h + 1) * HALF)
                if h == 0:
                    act.wait_ge(acc_ready, NCH * (b - 1))
                nc.scalar.activation(g[:, par, ts, 0, :], norm[:, ts, :], ACT.Relu).then_inc(ghi_done, 1)

            def batch(b, par, ln, last=False):
                for j in range(NCH - 1 if last else NCH):
                    if ln and j >= NCH - 2:
                        g_hi(b + 1, j - (NCH - 2), 1 - par)
                    c = NCH * b + j
                    relu_out(c - 1, (j - 1) % NCH, 2 * b + (j - 1) // 2)
                    u_hi(c, j)

            with act.Fori(0, B // 2 - 1) as i:
                batch(2 * i + 1, 1, True)
                batch(2 * i + 2, 0, True)
            batch(B - 1, 1, False, last=True)
            relu_out(LAST - 1, NCH - 2, (LAST - 1) // 2)
            for h in range(2):
                act.wait_ge(acc_ready, LAST + 1 + h)
                nc.scalar.activation(u16[:, 1, 0, h * HCW:(h + 1) * HCW], acc[:, (NCH - 1) * (1 - h), 0:HCW],
                                     ACT.Copy, scale=1.0 / U_DOWN).then_inc(u_hi_done, 1)
                act.wait_ge(uw_ready, LAST + 1 + 2 * h)
                act.wait_ge(stored[1], 16 * (LAST // 2))
                n = (NCH - 1) * BPC + 2 * h
                nc.scalar.activation(o_sb[:, 1, 2 * h, :], tp[:, 1 - h, 0:P], ACT.Relu, scale=y_out[:, n:n + 1]
                                     ).then_inc(relu_out_done, 1)

        @block.tensor
        def _(pe):
            def adj_transposes(k, i, j, n):
                use = use_of["T", k, i]
                if k == 0:
                    pe.wait_ge(piece_here[i], 32)
                elif i == 0:
                    pe.wait_ge(row_here[k % ROWS], 16 * row_loads(k))
                    if k + 1 < NB:
                        pe.wait_ge(col_here[k % COLS], 16 * col_loads(k))
                tp_free(pe, use)
                for b in range(n):
                    src = row_part(k, k, 1) if j + b == k else col_part(k, j + b)
                    t = nc.tensor.transpose(tp[:, use % 2, b * P:(b + 1) * P], src, ident[:, :])
                t.then_inc(adjT_ready, 1)

            def mat_transposes(k, i, j, n):
                c = f_before[k] + i
                if c >= 2:
                    pe.wait_ge(matT_stored, c - 1)
                for b in range(n):
                    for h in range(2):
                        t = nc.tensor.transpose(ft[:, c % 2, b, h, :], mat[:, k, h, (j + b) * P:(j + b + 1) * P],
                                                ident16[:, :])
                t.then_inc(matT_ready, 1)

            def column_sums(k):
                pe.wait_ge(lo_done, k + 1)
                use = use_of["C", k, 0]
                tp_free(pe, use)
                for j in range(k + 1, NB):
                    for h, ones in ((0, ones_hi), (1, ones_lo)):
                        m = nc.tensor.matmul(tp[:, use % 2, j:j + 1], mat[:, k, h, j * P:(j + 1) * P], ones[:, :],
                                             start=(h == 0), stop=(h == 1))
                m.then_inc(colsum_ready, 1)

            def products(m, j, par):
                cols = slice(j * CW, (j + 1) * CW)
                nc.tensor.matmul(acc[:, j, :], g[:, par, m, 0, :], mat[:, m, 0, cols], start=(m == 0), stop=False)
                nc.tensor.matmul(acc[:, j, :], g[:, par, m, 1, :], mat[:, m, 0, cols], start=False, stop=False)
                return nc.tensor.matmul(acc[:, j, :], g[:, par, m, 2, :], mat[:, m, 1, cols],
                                        start=False, stop=(m == NB - 1))

            def block_times_w(o, slot, n):
                nc.tensor.matmul(o, u16[:, slot, 0, n], w16[:, 0], start=True, stop=False)
                nc.tensor.matmul(o, u16[:, slot, 0, n], w16[:, 1], start=False, stop=False)
                return nc.tensor.matmul(o, u16[:, slot, 1, n], w16[:, 2], start=False, stop=True)

            def times_w(c, j, bank_used=True):
                pe.wait_ge(u_lo_done, c + 1)
                if bank_used:
                    pe.wait_ge(relu_out_done, c - 1)
                for t in range(BPC):
                    i = block_times_w(tp[:, j % 2, t * P:(t + 1) * P], j % 2, slice(t * P, (t + 1) * P))
                i.then_inc(uw_ready, 1)

            def last_times_w(h):
                pe.wait_ge(u_lo_done, LAST + 1 + h)
                pe.wait_ge(relu_out_done, LAST - 1 + h)
                for t, o in enumerate((tp[:, 1 - h, 0:P], acc[:, 1 + h, 0:P])):
                    block_times_w(o, 1, slice(h * HCW + t * P, h * HCW + (t + 1) * P)).then_inc(uw_ready, 1)

            def keep_warm(n):
                for _ in range(n):
                    nc.tensor.matmul(acc[:, 0, 0:P], ident16[:, :], ident16[:, :], start=True, stop=True)

            pe.wait_ge(ident_done, 1)
            pe.wait_ge(ident16_done, 1)
            pe.wait_ge(consts_done, 2)
            for s, step in enumerate(steps):
                if s == 1:
                    keep_warm(44)
                if s == 2:
                    keep_warm(50)
                for kind, k, i in step:
                    if kind == "T":
                        adj_transposes(k, i, *blocks_of(k)[i])
                    elif kind == "M":
                        mat_transposes(k, i, *blocks_of(k + 1)[i])
                    elif kind == "C":
                        column_sums(k)
                    else:
                        if i == 0:
                            if k >= 1:
                                pe.wait_ge(matT_stored, f_before[k - 1] + 1)
                            pe.wait_ge(glo2_done, k + 1)
                            pe.wait_ge(gneg2_done, k + 1)
                            pe.wait_ge(shell_done, k + 1)
                        last = products(k, i, 0)
                        if k == NB - 1:
                            last.then_inc(acc_ready, 1)
                            if i == 2:
                                pe.wait_ge(w_lo_done, 1)
                                pe.wait_ge(w_neg_done, 1)
                            if i >= 2:
                                times_w(i - 2, i - 2, bank_used=False)

            def batch(b, par, first=False, last=False):
                for j in range(NCH - 1 if last else NCH):
                    c = NCH * b + j
                    pe.wait_ge(u_lo_done, c - NCH + 1)
                    for m in range(NB):
                        if not first and j == 0 and m % HALF == 0:
                            pe.wait_ge(glo_done, 2 * (b - 2) + m // HALF + 1)
                            pe.wait_ge(gneg_done, 2 * (b - 2) + m // HALF + 1)
                        if first and j == 0 and m == 2:
                            times_w(c - 2, (j - 2) % NCH)
                        if m == HALF:
                            times_w(c - 1, (j - 1) % NCH)
                        done = products(m, j, par)
                    done.then_inc(acc_ready, 1)

            batch(1, 1, first=True)
            with pe.Fori(1, B // 2 - 1) as i:
                batch(2 * i, 0)
                batch(2 * i + 1, 1)
            batch(B - 2, 0)
            batch(B - 1, 1, last=True)

            for h in range(2):
                n0 = (NCH - 1) * CW + h * HCW
                bank = (NCH - 1) if h == 0 else 0
                pe.wait_ge(u_lo_done, LAST - NCH + 1 + h)
                for m in range(NB):
                    if m == HALF and h == 0:
                        times_w(LAST - 1, NCH - 2)
                    if m == HALF and h == 1:
                        last_times_w(0)
                    for i, (stationary, half) in enumerate(((0, 0), (1, 0), (2, 1))):
                        done = nc.tensor.matmul(acc[:, bank, 0:HCW], g[:, 1, m, stationary, :],
                                                mat[:, m, half, n0:n0 + HCW], start=(m == 0 and i == 0),
                                                stop=(m == NB - 1 and i == 2))
                done.then_inc(acc_ready, 1)
            last_times_w(1)


_INS = ['x', 'adj', 'L0_gnn_W']
_OUTS = [((8, 2048, 128), 'float32')]


def kernel(**inputs):
    import numpy as _np
    import concourse.bacc as _bacc
    from concourse import mybir as _mybir
    from concourse.bass_utils import run_bass_kernel_spmd as _run

    nc = _bacc.Bacc("TRN2", target_bir_lowering=False, num_devices=1)
    arrays, args = {}, []
    for name in _INS:
        a = _np.ascontiguousarray(inputs[name])
        arrays[f"in_{name}_dram"] = a
        args.append(nc.dram_tensor(f"in_{name}_dram", a.shape, _mybir.dt.from_np(a.dtype), kind="ExternalInput").ap())
    for i, (shape, dtype) in enumerate(_OUTS):
        dt = _mybir.dt.from_np(_np.dtype(dtype))
        args.append(nc.dram_tensor(f"out_{i}_dram", shape, dt, kind="ExternalOutput").ap())
    gnn_kernel(nc, *args)
    r = _run(nc, [arrays], core_ids=[0])
    got = tuple(r.results[0][f"out_{i}_dram"] for i in range(len(_OUTS)))
    return got[0]
```
